# Optimizing a Trainium2 kernel written in Bass

```python
import numpy as np
import jax
import jax.numpy as jnp

def _softmax(x, axis=-1):
    return jax.nn.softmax(x, axis=axis)
def _gelu(x):
    return jax.nn.gelu(x, approximate=True)
def _silu(x):
    return jax.nn.silu(x)
def _sigmoid(x):
    return jax.nn.sigmoid(x)
def _layernorm(x, axis=-1, eps=1e-5):
    m = jnp.mean(x, axis=axis, keepdims=True)
    v = jnp.var(x, axis=axis, keepdims=True)
    return (x - m) / jnp.sqrt(v + eps)
def _scatter_add(tgt, idx, src, axis=0):
    return tgt.at[idx].add(src)
def _segment_sum(src, seg, n):
    return jax.ops.segment_sum(src, seg, n)

kernel_name = 'mk_conv_preact_d2_conv_nhwc256_003c80'

def setup_inputs(seed: int = 0):
    np.random.seed(seed)
    _w = jnp.asarray
    def _rec_inputs():
        import jax
        import jax.numpy as jnp
        _gk = jax.random.key(seed)
        x = -0.000125 + 0.9999 * jax.random.normal(jax.random.fold_in(_gk, 1), (8, 128, 128, 256), jnp.float32)
        return x
    x = _rec_inputs()
    def _L0_conv_setup():
        import jax, jax.numpy as jnp
        import numpy as np
        B, H, W, C = (8, 128, 128, 256)
        K, DT, EPS = (5, 0.2, 0.001)
        LAM2 = 4.0

        def _dwconv(x, w):
            k = w.reshape(3, 3, 1, C)
            return jax.lax.conv_general_dilated(x, k, (1, 1), 'SAME', dimension_numbers=('NHWC', 'HWIO', 'NHWC'), feature_group_count=C)

        def _bn(x, gamma, beta, mean, var):
            return (x - mean) * jax.lax.rsqrt(var + EPS) * gamma + beta

        def _sobel(x):
            xp = jnp.pad(x, ((0, 0), (1, 1), (1, 1), (0, 0)), mode='reflect')
            top, mid, bot = (xp[:, :-2], xp[:, 1:-1], xp[:, 2:])
            gy = bot[:, :, :-2] + 2 * bot[:, :, 1:-1] + bot[:, :, 2:] - (top[:, :, :-2] + 2 * top[:, :, 1:-1] + top[:, :, 2:])
            gx = top[:, :, 2:] + 2 * mid[:, :, 2:] + bot[:, :, 2:] - (top[:, :, :-2] + 2 * mid[:, :, :-2] + bot[:, :, :-2])
            return (gy, gx)
        key = jax.random.key(seed)
        ks = jax.random.split(key, 6)
        f = jnp.float32
        d = {}
        d['s0'] = jax.random.normal(ks[0], (B, H, W, C), f)
        d['wg'] = jax.random.normal(ks[1], (3, 3, C), f) * 0.1
        d['wg1'] = jax.random.normal(ks[2], (3, 3, C), f) * 0.1
        for i, p in enumerate(['g', 'g1', 'out']):
            k4 = jax.random.split(ks[3 + i], 4)
            d[p + '_gamma'] = 1.0 + 0.1 * jax.random.normal(k4[0], (C,), f)
            d[p + '_beta'] = 0.1 * jax.random.normal(k4[1], (C,), f)
            d[p + '_mean'] = 0.1 * jax.random.normal(k4[2], (C,), f)
            d[p + '_var'] = 0.5 + jax.random.uniform(k4[3], (C,), f)
        return d
    _L0_conv_all = _L0_conv_setup()
    _L0_conv_in = {k: v for k, v in _L0_conv_all.items() if k in ('wg', 'wg1', 'g_gamma', 'g_beta', 'g_mean', 'g_var', 'g1_gamma', 'g1_beta', 'g1_mean', 'g1_var', 'out_gamma', 'out_beta', 'out_mean', 'out_var', )}
    del _L0_conv_all

    def _L1_conv_setup():
        import jax, jax.numpy as jnp
        import numpy as np
        NLAT, NLON = (128, 256)
        CIN, COUT = (128, 128)
        MODES_LAT, MODES_LON = (32, 32)
        BATCH = 4

        def _legendre(lmax, mmax, x):
            npts = x.shape[0]
            pct = np.zeros((lmax, mmax, npts), dtype=np.float64)
            s = np.sqrt(1.0 - x * x)
            pmm = np.full(npts, np.sqrt(1.0 / (4.0 * np.pi)))
            for m in range(mmax):
                if m < lmax:
                    pct[m, m] = pmm
                    if m + 1 < lmax:
                        pct[m + 1, m] = x * np.sqrt(2.0 * m + 3.0) * pmm
                    for l in range(m + 2, lmax):
                        a = np.sqrt((4.0 * l * l - 1.0) / (l * l - m * m))
                        b = np.sqrt(((l - 1.0) ** 2 - m * m) / (4.0 * (l - 1.0) ** 2 - 1.0))
                        pct[l, m] = a * (x * pct[l - 1, m] - b * pct[l - 2, m])
                pmm = pmm * -np.sqrt((2.0 * m + 3.0) / (2.0 * m + 2.0)) * s
            return pct
        key = jax.random.key(seed)
        k1, k2 = jax.random.split(key)
        x = jax.random.normal(k1, (BATCH, CIN, NLAT, NLON), dtype=jnp.float32)
        scale = 1.0 / (CIN * COUT)
        weights = scale * jax.random.normal(k2, (CIN, COUT, MODES_LAT, MODES_LON, 2), dtype=jnp.float32)
        theta = (np.arange(NLAT) + 0.5) * np.pi / NLAT
        ct = np.cos(theta)
        w = np.pi / NLAT * np.sin(theta)
        pct = _legendre(NLAT, NLON // 2 + 1, ct)
        return {'x': x, 'weights': weights, 'pct': jnp.asarray(pct, jnp.float32), 'w': jnp.asarray(w, jnp.float32)}
    _L1_conv_all = _L1_conv_setup()
    _L1_conv_in = {k: v for k, v in _L1_conv_all.items() if k in ('weights', 'pct', 'w', )}
    del _L1_conv_all

    return {
        "x": x,
        "L0_conv_wg": _L0_conv_in["wg"],
        "L0_conv_wg1": _L0_conv_in["wg1"],
        "L0_conv_g_gamma": _L0_conv_in["g_gamma"],
        "L0_conv_g_beta": _L0_conv_in["g_beta"],
        "L0_conv_g_mean": _L0_conv_in["g_mean"],
        "L0_conv_g_var": _L0_conv_in["g_var"],
        "L0_conv_g1_gamma": _L0_conv_in["g1_gamma"],
        "L0_conv_g1_beta": _L0_conv_in["g1_beta"],
        "L0_conv_g1_mean": _L0_conv_in["g1_mean"],
        "L0_conv_g1_var": _L0_conv_in["g1_var"],
        "L0_conv_out_gamma": _L0_conv_in["out_gamma"],
        "L0_conv_out_beta": _L0_conv_in["out_beta"],
        "L0_conv_out_mean": _L0_conv_in["out_mean"],
        "L0_conv_out_var": _L0_conv_in["out_var"],
        "L1_conv_weights": _L1_conv_in["weights"],
        "L1_conv_pct": _L1_conv_in["pct"],
        "L1_conv_w": _L1_conv_in["w"],
    }

def reference(x, L0_conv_wg, L0_conv_wg1, L0_conv_g_gamma, L0_conv_g_beta, L0_conv_g_mean, L0_conv_g_var, L0_conv_g1_gamma, L0_conv_g1_beta, L0_conv_g1_mean, L0_conv_g1_var, L0_conv_out_gamma, L0_conv_out_beta, L0_conv_out_mean, L0_conv_out_var, L1_conv_weights, L1_conv_pct, L1_conv_w):
    import jax
    import jax.numpy as jnp
    def _L0_conv_ref(s0, wg, wg1, g_gamma, g_beta, g_mean, g_var, g1_gamma, g1_beta, g1_mean, g1_var, out_gamma, out_beta, out_mean, out_var):
        import jax, jax.numpy as jnp
        import numpy as np
        B, H, W, C = (8, 128, 128, 256)
        K, DT, EPS = (5, 0.2, 0.001)
        LAM2 = 4.0

        def _dwconv(x, w):
            k = w.reshape(3, 3, 1, C)
            return jax.lax.conv_general_dilated(x, k, (1, 1), 'SAME', dimension_numbers=('NHWC', 'HWIO', 'NHWC'), feature_group_count=C)

        def _bn(x, gamma, beta, mean, var):
            return (x - mean) * jax.lax.rsqrt(var + EPS) * gamma + beta

        def _sobel(x):
            xp = jnp.pad(x, ((0, 0), (1, 1), (1, 1), (0, 0)), mode='reflect')
            top, mid, bot = (xp[:, :-2], xp[:, 1:-1], xp[:, 2:])
            gy = bot[:, :, :-2] + 2 * bot[:, :, 1:-1] + bot[:, :, 2:] - (top[:, :, :-2] + 2 * top[:, :, 1:-1] + top[:, :, 2:])
            gx = top[:, :, 2:] + 2 * mid[:, :, 2:] + bot[:, :, 2:] - (top[:, :, :-2] + 2 * mid[:, :, :-2] + bot[:, :, :-2])
            return (gy, gx)
        fsrc = s0
        h = s0
        h0 = fsrc
        g = jax.nn.relu(_bn(_dwconv(h, wg), g_gamma, g_beta, g_mean, g_var))
        g1 = jax.nn.relu(_bn(_dwconv(h, wg1), g1_gamma, g1_beta, g1_mean, g1_var))
        gy, gx = _sobel(h)
        Dx = 1.0 / (gy * gy / LAM2 + 1.0)
        Dy = 1.0 / (gx * gx / LAM2 + 1.0)
        ux = 0.5 * (jnp.roll(g, 1, axis=2) - jnp.roll(g, -1, axis=2))
        vy = 0.5 * (jnp.roll(g1, 1, axis=3) - jnp.roll(g1, -1, axis=3))
        Ax, Ay = (g * DT, g1 * DT)
        Bx, By = (Dx * DT, Dy * DT)
        E = (ux + vy) * DT
        D = 1.0 / (1.0 + 2.0 * Bx + 2.0 * By)
        cm_x, cp_x = (-Ax + 2.0 * Bx, Ax + 2.0 * Bx)
        cm_y, cp_y = (-Ay + 2.0 * By, Ay + 2.0 * By)
        c0 = 1.0 - 2.0 * Bx - 2.0 * By
        for _ in range(K):
            prev = h
            h = D * (c0 * h0 - 2.0 * E * h + cm_x * jnp.roll(h, 1, axis=2) + cp_x * jnp.roll(h, -1, axis=2) + cm_y * jnp.roll(h, 1, axis=3) + cp_y * jnp.roll(h, -1, axis=3))
            h = h + D * (2.0 * DT) * fsrc
            h0 = prev
        return jax.nn.relu(_bn(h, out_gamma, out_beta, out_mean, out_var))

    def _L1_conv_ref(x, weights, pct, w):
        import jax, jax.numpy as jnp
        import numpy as np
        NLAT, NLON = (128, 256)
        CIN, COUT = (128, 128)
        MODES_LAT, MODES_LON = (32, 32)
        BATCH = 4

        def _legendre(lmax, mmax, x):
            npts = x.shape[0]
            pct = np.zeros((lmax, mmax, npts), dtype=np.float64)
            s = np.sqrt(1.0 - x * x)
            pmm = np.full(npts, np.sqrt(1.0 / (4.0 * np.pi)))
            for m in range(mmax):
                if m < lmax:
                    pct[m, m] = pmm
                    if m + 1 < lmax:
                        pct[m + 1, m] = x * np.sqrt(2.0 * m + 3.0) * pmm
                    for l in range(m + 2, lmax):
                        a = np.sqrt((4.0 * l * l - 1.0) / (l * l - m * m))
                        b = np.sqrt(((l - 1.0) ** 2 - m * m) / (4.0 * (l - 1.0) ** 2 - 1.0))
                        pct[l, m] = a * (x * pct[l - 1, m] - b * pct[l - 2, m])
                pmm = pmm * -np.sqrt((2.0 * m + 3.0) / (2.0 * m + 2.0)) * s
            return pct
        b, cin, nlat, nlon = x.shape
        mmax = nlon // 2 + 1
        xf = jnp.fft.rfft(x, axis=-1) * (2.0 * jnp.pi / nlon)
        x_spec = jnp.einsum('lmt,bctm->bclm', pct * w, xf)
        wc = (weights[..., 0] + 1j * weights[..., 1]).astype(jnp.complex64)
        ml = min(MODES_LAT, nlat)
        mj = min(MODES_LON, mmax)
        out_block = jnp.einsum('bilm,iolm->bolm', x_spec[:, :, :ml, :mj], wc[:, :, :ml, :mj])
        out_spec = jnp.zeros((b, wc.shape[1], nlat, mmax), jnp.complex64)
        out_spec = out_spec.at[:, :, :ml, :mj].set(out_block)
        xf_out = jnp.einsum('lmt,bclm->bctm', pct, out_spec)
        out = jnp.fft.irfft(xf_out, n=nlon, axis=-1) * nlon
        return out

    def _gn(v, G=32, eps=1e-5):
        B_, H_, W_, C_ = v.shape
        g = v.reshape(B_, H_, W_, G, C_ // G)
        m = jnp.mean(g, axis=(1, 2, 4), keepdims=True)
        s = jnp.var(g, axis=(1, 2, 4), keepdims=True)
        return ((g - m) / jnp.sqrt(s + eps)).reshape(v.shape)

    def _ln_c(v, eps=1e-6):
        m = jnp.mean(v, axis=-1, keepdims=True)
        s = jnp.var(v, axis=-1, keepdims=True)
        return (v - m) / jnp.sqrt(s + eps)

    def _ln_t(v, eps=1e-5):
        m = jnp.mean(v, axis=-1, keepdims=True)
        s = jnp.var(v, axis=-1, keepdims=True)
        return (v - m) / jnp.sqrt(s + eps)

    def _to_tokens(v):
        B_, H_, W_, C_ = v.shape
        return v.reshape(B_, H_ * W_, C_)
    def _from_tokens(t, like):
        return t.reshape(like.shape)

    x = x + _L0_conv_ref(_gn(x), L0_conv_wg, L0_conv_wg1, L0_conv_g_gamma, L0_conv_g_beta, L0_conv_g_mean, L0_conv_g_var, L0_conv_g1_gamma, L0_conv_g1_beta, L0_conv_g1_mean, L0_conv_g1_var, L0_conv_out_gamma, L0_conv_out_beta, L0_conv_out_mean, L0_conv_out_var)
    x = x + _L1_conv_ref(_gn(x), L1_conv_weights, L1_conv_pct, L1_conv_w)
    return x


_drawn_inputs = setup_inputs


def setup_inputs(seed=0):
    import zlib

    import numpy as np

    out = dict(_drawn_inputs(seed))
    spreads = {}
    factors = {'L0_conv_g_gamma': 7.82,
     'L0_conv_g_beta': 3.281,
     'L0_conv_g_mean': 3.018,
     'L0_conv_g_var': 4.227,
     'L0_conv_g1_gamma': 8.0,
     'L0_conv_g1_beta': 3.06,
     'L0_conv_g1_mean': 3.06,
     'L0_conv_g1_var': 5.207,
     'L1_conv_weights': 8.0,
     'L1_conv_pct': 8.0,
     'L1_conv_w': 8.0}
    for name, (base, spread) in spreads.items():
        noise = np.random.default_rng([zlib.crc32(name.encode()), seed]).standard_normal(out[name].shape)
        drawn = base * np.exp(spread * noise) if base else spread * noise
        out[name] = jnp.asarray(drawn.astype(out[name].dtype))
    for name, factor in factors.items():
        out[name] = (out[name] * factor).astype(out[name].dtype)
    return out
```

```python
from contextlib import ExitStack

import numpy as np

import concourse.bass as bass
from concourse import mybir

F32 = mybir.dt.float32
BF16 = mybir.dt.bfloat16
ALU = mybir.AluOpType
ACT = mybir.ActivationFunctionType

P = 128
NLON = 256
HALF = NLON // 2
MODES = 32
RG = 4
SAMPLE_ROWS = 128
GPS = SAMPLE_ROWS // RG
GPS_BITS = GPS.bit_length() - 1
GC = 8
STEPS = 5
DT = 0.2
BN_EPS = 1e-3
GN_EPS = 1e-5
CB = 32
NB_ = NLON // CB


def shape_constants():
    i = np.arange(P)
    eye = np.eye(P, dtype=np.float32)
    prev, nxt = (i - 1) % P, (i + 1) % P
    from_next = np.zeros((P, P), np.float32)
    from_next[nxt, i] = 1
    from_prev = np.zeros((P, P), np.float32)
    from_prev[prev, i] = 1
    lo, hi = np.abs(i - 1), (P - 1) - np.abs((P - 1) - (i + 1))
    smooth = np.zeros((P, P), np.float32)
    slope = np.zeros((P, P), np.float32)
    for w in range(P):
        smooth[lo[w], w] += 1
        smooth[w, w] += 2
        smooth[hi[w], w] += 1
        slope[hi[w], w] += 1
        slope[lo[w], w] -= 1
    mats = {
        "eye": eye, "minus_eye": -eye, "source": -2 * DT * eye,
        "from_next": from_next, "from_prev": from_prev,
        "prev_minus_next": from_prev - from_next,
        "smooth": smooth, "minus_smooth": -smooth, "slope": slope, "slope2": 2 * slope,
        "block_mean": np.kron(np.eye(P // GC), np.full((GC, GC), 1.0 / GC)).astype(np.float32),
        "ones": np.ones((P, P), np.float32),
        "row_pick": np.isin(i, (0, 32, 64)).astype(np.float32)[:, None] * np.ones((1, P), np.float32),
    }
    channel_mask = (i[:, None] % CB == np.arange(CB)[None]).astype(np.float32)
    row_mask = np.ones((P, 2, GPS + 1), np.float32)
    row_mask[0:CB, 0, 0] = row_mask[0:CB, 0, GPS] = 0
    row_mask[P - CB:P, 1, GPS - 1] = 0
    n, m = np.arange(NLON), np.arange(MODES)
    ang = 2 * np.pi * np.outer(n, m) / NLON
    dft = np.concatenate([np.cos(ang), -np.sin(ang)], 1) * (2 * np.pi / NLON)
    dft = dft.reshape(2, HALF, 2 * MODES).transpose(1, 0, 2)
    both = np.where(m == 0, 1.0, 2.0)[:, None]
    idft = np.concatenate([both * np.cos(ang.T), -both * np.sin(ang.T)], 0)
    return {
        "mats": np.stack(list(mats.values()), 1).astype(np.float32),
        "channel_mask": channel_mask,
        "row_mask": row_mask,
        "dft": np.ascontiguousarray(dft, dtype=np.float32),
        "idft": np.concatenate([idft, idft], 0).astype(np.float32),
    }, list(mats)


def newton_rsqrt(nc, dve, act, chain, out, var, eps, tmp, sqrt_done, add_done):
    if dve is None:
        act.wait_ge(add_done[0], add_done[1])
        nc.scalar.activation(out, var, ACT.Sqrt).then_inc(sqrt_done[0], 1)
        return
    chain(nc.vector.tensor_scalar(var, var, eps, None, ALU.add), add_done[0])
    dve.wait_ge(sqrt_done[0], sqrt_done[1])
    chain(nc.vector.reciprocal(out, out))
    chain(nc.vector.tensor_tensor(tmp, out, out, ALU.mult))
    chain(nc.vector.tensor_tensor(tmp, tmp, var, ALU.mult))
    chain(nc.vector.tensor_scalar(tmp, tmp, -0.5, 1.5, ALU.mult, ALU.add))
    chain(nc.vector.tensor_tensor(out, out, tmp, ALU.mult))


def build(nc, x, wg, wg1, g_gamma, g_beta, g_mean, g_var, g1_gamma, g1_beta, g1_mean, g1_var,
          o_gamma, o_beta, o_mean, o_var, weights, pct, quad_w,
          c_mats, c_channel_mask, c_row_mask, c_dft, c_idft, mat_names, y):
    B = x.shape[0]
    ROWS = B * SAMPLE_ROWS
    NG = ROWS // RG
    assert x.shape[1:] == (P, P, NLON)

    x_rows = x.rearrange("b h w c -> (b h) w c").rearrange("r w c -> w r c")
    y_rows = y.rearrange("b h w c -> (b h) w c").rearrange("r w c -> w r c")
    x1 = nc.dram_tensor("x1_scratch", (ROWS, P, NLON), F32).ap()
    x1_rows = x1.rearrange("r w c -> w r c")

    with ExitStack() as kernel_scope:
        def alloc(scope):
            def sb(name, shape, dt=F32):
                return scope.enter_context(nc.sbuf_tensor(name, shape, dt))

            def ps(name, shape):
                return scope.enter_context(nc.psum_tensor(name, shape, F32))

            def sem(name):
                return scope.enter_context(nc.semaphore(name))
            return sb, ps, sem

        sb, _, _ = alloc(kernel_scope)
        mats = sb("mats", [P, len(mat_names), P])
        gn_scale = sb("gn_scale", [P, B, 2])
        gn_bias = sb("gn_bias", [P, B, 2])
        stats_scope = ExitStack()
        stats = stats_scope.enter_context(nc.sbuf_tensor("stats", [P, 2 * ROWS // 2, 6], F32))

        def mat(name):
            return mats[:, mat_names.index(name), :]

        def stats_index(n, half):
            return n + half * NG

        with ExitStack() as scope:
            sb, ps, sem = alloc(scope)
            NR = 4
            rows = [sb(f"stat_rows{i}", [P, RG, NLON]) for i in range(NR)]
            turned = [ps(f"stat_turned{i}", [P, 2, RG * P]) for i in range(2)]
            mats_loaded = sem("mats_loaded")
            rows_loaded = [sem(f"rows_loaded{i}") for i in range(NR)]
            rows_turned, stats_taken = sem("rows_turned"), sem("stats_taken")
            block = scope.enter_context(nc.Block(name="stats"))

            @block.sync
            def _(sp):
                sp.dma_start(mats[:], c_mats).then_inc(mats_loaded, 16)
                for i in range(NR):
                    sp.dma_start(rows[i][:], x_rows[:, i * RG:(i + 1) * RG, :]).then_inc(rows_loaded[i], 16)
                with sp.Fori(0, NG // NR - 1) as t:
                    for i in range(NR):
                        sp.wait_ge(rows_turned, t * NR + i + 1)
                        sp.dma_start(rows[i][:], x_rows[:, bass.ds((t * NR + NR + i) * RG, RG), :]) \
                            .then_inc(rows_loaded[i], 16)

            @block.tensor
            def _(pe):
                pe.wait_ge(mats_loaded, 16)
                with pe.Fori(0, NG // NR) as t:
                    for i in range(NR):
                        pe.wait_ge(rows_loaded[i], t * 16 + 16)
                        pe.wait_ge(stats_taken, t * (2 * NR) + max(2 * i - 2, 0))
                        for r in range(RG):
                            for h in range(2):
                                mm = nc.tensor.transpose(turned[i % 2][:, h, r * P:(r + 1) * P],
                                                         rows[i][:, r, h * HALF:(h + 1) * HALF], mat("eye"))
                        mm.then_inc(rows_turned, 1)

            @block.vector
            def _(dve):
                with dve.Fori(0, NG // 2) as t:
                    for i in range(2):
                        dve.wait_ge(rows_turned, t * 2 + i + 1)
                        for h in range(2):
                            nc.vector.bn_stats(
                                out=stats[:, bass.ds(stats_index(t * 2 + i, h), 1), :].rearrange("p a k -> p (a k)"),
                                in_=turned[i][:, h, :]).then_inc(stats_taken, 1)

        def group_norm_scales(tag, per_sample):
            with ExitStack() as scope:
                sb, ps, sem = alloc(scope)
                mv = sb(f"mv{tag}", [P, B * 2, 2])
                moments = sb(f"moments{tag}", [P, 2, B * 2])
                group_m = ps(f"group_m{tag}", [P, 2, B * 2])
                gm = sb(f"gm{tag}", [P, 2, B * 2])
                var = sb(f"var{tag}", [P, B * 2])
                tmp = sb(f"tmp{tag}", [P, B * 2])
                step, var_ready, sqrt_done = sem(f"step{tag}"), sem(f"var_ready{tag}"), sem(f"sqrt_done{tag}")
                moments_ready, group_ready = sem(f"moments_ready{tag}"), sem(f"group_ready{tag}")
                scale = gn_scale[:].rearrange("p b h -> p (b h)")
                bias = gn_bias[:].rearrange("p b h -> p (b h)")
                block = scope.enter_context(nc.Block(name=f"norm{tag}"))

                @block.vector
                def _(dve):
                    n = [0]

                    def chain(ins, other=None):
                        if other is not None:
                            ins.then_inc(other, 1)
                            dve.wait_ge(other, 1)
                            return
                        n[0] += 1
                        ins.then_inc(step, 1)
                        dve.wait_ge(step, n[0])

                    for k in range(2 * B):
                        first = ((k % 2) * B + k // 2) * per_sample
                        ins = nc.vector.bn_aggr(
                            out=mv[:, k, :], in_=stats[:, first:first + per_sample, :].rearrange("p a k -> p (a k)"))
                    chain(ins)
                    chain(nc.vector.tensor_copy(moments[:, 0, :], mv[:, :, 0]))
                    chain(nc.vector.tensor_tensor(moments[:, 1, :], mv[:, :, 0], mv[:, :, 0], ALU.mult))
                    chain(nc.vector.tensor_tensor(moments[:, 1, :], moments[:, 1, :], mv[:, :, 1], ALU.add), moments_ready)
                    dve.wait_ge(group_ready, 1)
                    chain(nc.vector.tensor_copy(gm[:], group_m[:]))
                    chain(nc.vector.tensor_tensor(tmp[:], gm[:, 0, :], gm[:, 0, :], ALU.mult))
                    chain(nc.vector.tensor_tensor(var[:], gm[:, 1, :], tmp[:], ALU.subtract))
                    chain(nc.vector.tensor_scalar(var[:], var[:], 0.0, None, ALU.max))
                    newton_rsqrt(nc, dve, None, chain, scale, var[:], GN_EPS, tmp[:],
                                 (sqrt_done, 1), (var_ready, 1))
                    chain(nc.vector.scalar_tensor_tensor(out=bias, in0=gm[:, 0, :], scalar=-1.0, in1=scale,
                                                         op0=ALU.mult, op1=ALU.mult))

                @block.tensor
                def _(pe):
                    pe.wait_ge(moments_ready, 1)
                    nc.tensor.matmul(group_m[:].rearrange("p a k -> p (a k)"), mat("block_mean"),
                                     moments[:].rearrange("p a k -> p (a k)"), start=True, stop=True) \
                        .then_inc(group_ready, 1)

                @block.scalar
                def _(act):
                    newton_rsqrt(nc, None, act, None, scale, var[:], GN_EPS, None, (sqrt_done, 1), (var_ready, 1))

        group_norm_scales("_x", GPS)

        with ExitStack() as scope:
            sb, ps, sem = alloc(scope)
            conv_w = sb("conv_w", [P, NB_, 3, 2, 2, CB])
            conv_bias = sb("conv_bias", [P, 2, 2, 2, HALF], BF16)
            row_pick = sb("row_pick", [P, P], BF16)
            norm_scale = sb("norm_scale", [P, B + 1, NLON])
            norm_bias = sb("norm_bias", [P, B + 1, NLON])
            out_scale = sb("out_scale", [P, NLON])
            out_bias = sb("out_bias", [P, NLON])
            row_mask = sb("row_mask", [P, 2, GPS + 1])

            with ExitStack() as prep:
                sb2, ps2, sem2 = alloc(prep)
                taps = sb2("taps", [P, 2, 3, 3, NLON])
                bn = sb2("bn", [P, 3, 4, NLON])
                bn_scale = sb2("bn_scale", [P, 3, NLON])
                bn_bias = sb2("bn_bias", [P, 3, NLON])
                tmp = sb2("bn_tmp", [P, 3, NLON])
                part = sb2("bias_part", [P, 3, 2, NLON], BF16)
                rest = sb2("bias_rest", [P, 2, NLON])
                channel_mask = sb2("channel_mask", [P, CB])
                diag = sb2("diag", [P, 4, HALF])
                spread = ps2("spread", [P, 2, NLON])
                loaded, step = sem2("prep_loaded"), sem2("prep_step")
                var_ready, sqrt_done = sem2("prep_var_ready"), sem2("prep_sqrt_done")
                diag_ready, spread_ready, spread_copied = sem2("diag_ready"), sem2("spread_ready"), sem2("spread_copied")
                block = prep.enter_context(nc.Block(name="prep"))
                params = (g_gamma, g_beta, g_mean, g_var, g1_gamma, g1_beta, g1_mean, g1_var,
                          o_gamma, o_beta, o_mean, o_var)
                LOADS = 2 + len(params) + 2

                @block.sync
                def _(sp):
                    for k, w in enumerate((wg, wg1)):
                        sp.dma_start(taps[:, k].rearrange("p a b c -> p (a b c)"),
                                     w.rearrange("a b c -> (a b c)").partition_broadcast(P)).then_inc(loaded, 16)
                    for k, v in enumerate(params):
                        sp.dma_start(bn[:, k // 4, k % 4, :], v.partition_broadcast(P)).then_inc(loaded, 16)
                    sp.dma_start(channel_mask[:], c_channel_mask).then_inc(loaded, 16)
                    sp.dma_start(row_mask[:], c_row_mask).then_inc(loaded, 16)

                @block.scalar
                def _(act):
                    newton_rsqrt(nc, None, act, None, bn_scale[:], bn[:, :, 3, :], BN_EPS, None,
                                 (sqrt_done, 1), (var_ready, 1))

                @block.vector
                def _(dve):
                    n = [0]

                    def chain(ins, other=None):
                        if other is not None:
                            ins.then_inc(other, 1)
                            dve.wait_ge(other, 1)
                            return
                        n[0] += 1
                        ins.then_inc(step, 1)
                        dve.wait_ge(step, n[0])

                    chain(nc.vector.memset(conv_w[:], 0.0))
                    chain(nc.vector.memset(conv_bias[:], 0.0))
                    chain(nc.vector.tensor_copy(row_pick[:], mat("row_pick")))
                    dve.wait_ge(loaded, 16 * LOADS)
                    newton_rsqrt(nc, dve, None, chain, bn_scale[:], bn[:, :, 3, :], BN_EPS, tmp[:],
                                 (sqrt_done, 1), (var_ready, 1))
                    chain(nc.vector.tensor_tensor(bn_scale[:], bn_scale[:], bn[:, :, 0, :], ALU.mult))
                    chain(nc.vector.tensor_tensor(tmp[:], bn_scale[:], bn[:, :, 2, :], ALU.mult))
                    chain(nc.vector.tensor_tensor(bn_bias[:], bn[:, :, 1, :], tmp[:], ALU.subtract))
                    chain(nc.vector.tensor_scalar(bn_scale[:, 0:2], bn_scale[:, 0:2], DT, None, ALU.mult))
                    chain(nc.vector.tensor_scalar(bn_bias[:, 0:2], bn_bias[:, 0:2], DT, None, ALU.mult))
                    chain(nc.vector.tensor_copy(out_scale[:], bn_scale[:, 2, :]))
                    chain(nc.vector.tensor_copy(out_bias[:], bn_bias[:, 2, :]))
                    for k in range(2):
                        for dy in range(3):
                            chain(nc.vector.tensor_tensor(
                                taps[:, k, dy], taps[:, k, dy],
                                bn_scale[:, k, :].unsqueeze(1).broadcast_to((P, 3, NLON)), ALU.mult))
                    for r in range(4):
                        q = slice(CB * r, CB * (r + 1))
                        for ro in range(2):
                            if not 0 <= r - ro <= 2:
                                continue
                            for k in range(2):
                                for dx in range(3):
                                    ins = nc.vector.tensor_tensor(
                                        conv_w[q, :, dx, k, ro, :],
                                        taps[q, k, r - ro, dx, :].rearrange("p (g c) -> p g c", c=CB),
                                        channel_mask[q, :].unsqueeze(1).broadcast_to((CB, NB_, CB)), ALU.mult)
                        chain(ins)
                    chain(nc.vector.tensor_copy(part[:, 0], bn_bias[:, 0:2]))
                    chain(nc.vector.tensor_tensor(rest[:], bn_bias[:, 0:2], part[:, 0], ALU.subtract))
                    chain(nc.vector.tensor_copy(part[:, 1], rest[:]))
                    chain(nc.vector.tensor_tensor(rest[:], rest[:], part[:, 1], ALU.subtract))
                    chain(nc.vector.tensor_copy(part[:, 2], rest[:]))
                    for j in range(3):
                        q = slice(CB * j, CB * (j + 1))
                        for h in range(2):
                            for ro in range(2):
                                ins = nc.vector.tensor_copy(conv_bias[q, h, :, ro, :],
                                                            part[q, j, :, h * HALF:(h + 1) * HALF])
                        chain(ins)
                    for b in range(B + 1):
                        if b >= 1:
                            dve.wait_ge(spread_ready, b)
                            chain(nc.vector.tensor_copy(norm_scale[:, b - 1, :], spread[:, 0, :]))
                            chain(nc.vector.tensor_copy(norm_bias[:, b - 1, :], spread[:, 1, :]))
                        if b == B:
                            break
                        for k, v in enumerate((gn_scale, gn_bias)):
                            for h in range(2):
                                ins = nc.vector.tensor_scalar(diag[:, 2 * k + h, :], mat("eye"), v[:, b, h:h + 1],
                                                              None, ALU.mult)
                        ins.then_inc(diag_ready, 1)
                    chain(nc.vector.tensor_copy(norm_scale[:, B, :], norm_scale[:, 0, :]))
                    chain(nc.vector.tensor_copy(norm_bias[:, B, :], norm_bias[:, 0, :]))

                @block.tensor
                def _(pe):
                    for b in range(B):
                        pe.wait_ge(diag_ready, b + 1)
                        for k in range(4):
                            mm = nc.tensor.matmul(spread[:].rearrange("p a c -> p (a c)")[:, k * HALF:(k + 1) * HALF],
                                                  mat("ones"), diag[:, k, :], start=True, stop=True)
                        mm.then_inc(spread_ready, 1)

            W2 = NLON + 2
            UR = 2
            NU = ROWS // UR
            x6 = sb("x6", [P, RG + 2, NLON])
            s6 = sb("s6", [P, RG + 2, NLON])
            x2 = [sb(f"x2_{i}", [P, UR, NLON]) for i in range(2)]
            x1_tile = [sb(f"x1_tile{i}", [P, UR, NLON]) for i in range(2)]
            f = [sb(f"f{i}", [P, UR, W2]) for i in range(2)]
            blocks4 = sb("blocks4", [P, NB_, 4, CB])
            convin = sb("convin", [P, NB_, P + 2])
            ab = sb("ab", [P, 2, RG, W2])
            row_sum = sb("row_sum", [P, RG, NLON])
            q2 = sb("q2", [P, 2, RG, NLON])
            unit_shape = [P, UR, NLON]
            pair_shape = [P, 2, UR, NLON]
            v, pm, rcp, tnewton, one_minus_d = (sb(k, unit_shape) for k in ("v", "pm", "rcp", "tnewton", "one_minus_d"))
            xy = sb("xy", pair_shape)
            minus_dab = sb("minus_dab", pair_shape)
            co = [{k: sb(f"co{i}_{k}", [P, 2] + pair_shape[1:] if k == "cross" else unit_shape) for k in
                   ("cross", "self", "old", "first", "src")} for i in range(2)]
            prod_w = sb("prod_w", pair_shape)
            prod_c = sb("prod_c", pair_shape)
            prod_self = sb("prod_self", unit_shape)
            m_old = [sb(f"m_old{i}", unit_shape) for i in range(2)]
            hbuf = [sb(f"h{i}", [P, UR, W2]) for i in range(2)]
            minus_04 = sb("minus_04", [P, 1])

            turn = ps("turn", [P, 4, P])
            cbank = ps("cbank", [P, 2, 2, UR, HALF])
            sbank = ps("sbank", [P, 2, UR, NLON])
            kbank = ps("kbank", unit_shape)
            hbank = ps("hbank", [P, 2, UR, NLON])

            names = """x6_loaded norm_step blocks_ready turned convin_ready conv_done
                relu_done pads_ab sobel_done squares_done v_ready pm_ready ln_done rcp0_ready coef_step
                old_ready self_done shift_done shifted_ready f_ready products accumulated
                h_ready last_step x1_turned x1_stats padded""".split()
            S = {k: sem(k) for k in names}
            x2_loaded = [sem(f"x2_loaded{i}") for i in range(2)]
            x1_stored = [sem(f"x1_stored{i}") for i in range(2)]
            block = scope.enter_context(nc.Block(name="layer0"))

            NORM = 3
            COEF = 11
            PRODUCTS = {k: 4 if k == 1 else 6 for k in range(1, STEPS + 1)}
            UNIT_PRODUCTS = sum(PRODUCTS.values())
            inner = slice(1, NLON + 1)

            def norm_count(j, i):
                return (j // 2 if isinstance(j, int) else j >> 1) * NORM + i

            def product_count(j, k, i=None):
                return j * UNIT_PRODUCTS + sum(PRODUCTS[a] for a in range(1, k)) + (PRODUCTS[k] if i is None else i)

            def h_count(j, k, i=3):
                return j * (3 * (STEPS - 1)) + 3 * (k - 1) + i

            def neighbours(h):
                ap = h[:]
                return bass.AP(tensor=ap.tensor, offset=ap.offset, ap=[list(ap.ap[0]), [2, 2], [W2, UR], [1, NLON]])

            def half_rows(ap, q):
                return ap[:, UR * q:UR * (q + 1)]

            @block.sync
            def _(sp):
                def load6(n, above, below):
                    for a, r in ((slice(1, RG + 1), bass.ds(n * RG, RG)), (slice(0, 1), bass.ds(above, 1)), (slice(RG + 1, RG + 2), bass.ds(below, 1))):
                        sp.dma_start(x6[:, a, :], x_rows[:, r, :]).then_inc(S["x6_loaded"], 16)

                for a, r in ((slice(1, RG + 1), 0), (slice(0, 1), 1), (slice(RG + 1, RG + 2), RG)):
                    sp.dma_start(x6[:, a, :], x_rows[:, r:r + a.stop - a.start, :]).then_inc(S["x6_loaded"], 16)
                sp.wait_ge(S["norm_step"], 1)
                for a, r in ((slice(1, RG + 1), RG), (slice(0, 1), RG - 1), (slice(RG + 1, RG + 2), 2 * RG)):
                    sp.dma_start(x6[:, a, :], x_rows[:, r:r + a.stop - a.start, :]).then_inc(S["x6_loaded"], 16)
                with sp.Fori(0, NG) as t:
                    n = (t + 2) & (NG - 1)
                    first = 1 - (((n & (GPS - 1)) + GPS - 1) >> GPS_BITS)
                    final = ((n & (GPS - 1)) + 1) >> GPS_BITS
                    above = sp.snap((n * RG - 1 + 2 * first).with_bounds(min_val=0, max_val=ROWS - 1))
                    below = sp.snap((n * RG + RG - 2 * final).with_bounds(min_val=0, max_val=ROWS - 1))
                    for p in range(2):
                        sp.wait_ge(S["last_step"], (t * 2 + p) * 3)
                        if p == 0:
                            sp.wait_ge(S["norm_step"], (t + 1) * NORM + 1)
                        sp.dma_start(x2[p][:], x_rows[:, bass.ds(t * RG + UR * p, UR), :]).then_inc(x2_loaded[p], 16)
                        if p == 0:
                            load6(n, above, below)
                        sp.wait_ge(S["last_step"], (t * 2 + p) * 3 + 3)
                        sp.dma_start(x1_rows[:, bass.ds(t * RG + UR * p, UR), :], x1_tile[p][:]).then_inc(x1_stored[p], 16)
                for p in range(2):
                    sp.wait_ge(x1_stored[p], 16 * NG)
                sp.wait_ge(S["x6_loaded"], 48 * (NG + 2))

            @block.vector
            def _(dve):
                def tt(out, a, b, op, done):
                    nc.vector.tensor_tensor(out, a, b, op).then_inc(done, 1)

                def stt(out, a, c, b, op0, op1, done, **kw):
                    nc.vector.scalar_tensor_tensor(out=out, in0=a, scalar=c, in1=b, op0=op0, op1=op1, **kw).then_inc(done, 1)

                def norm_scaled(n, sample):
                    dve.wait_ge(S["x6_loaded"], n * 48 + 48)
                    dve.wait_ge(S["sobel_done"], n * 2)
                    dve.wait_ge(S["blocks_ready"], n * 2)
                    dve.wait_ge(S["f_ready"], n * 6)
                    tt(s6[:], x6[:], norm_scale[:, bass.ds(sample, 1), :].broadcast_to((P, RG + 2, NLON)), ALU.mult, S["norm_step"])

                def norm_shifted(n, sample):
                    dve.wait_ge(S["norm_step"], n * NORM + 1)
                    tt(s6[:], s6[:], norm_bias[:, bass.ds(sample, 1), :].broadcast_to((P, RG + 2, NLON)), ALU.add, S["norm_step"])
                    dve.wait_ge(S["norm_step"], n * NORM + 2)
                    tt(row_sum[:], s6[:, 0:RG], s6[:, 2:RG + 2], ALU.add, S["norm_step"])

                def denominator(j, q, used=None):
                    dve.wait_ge(S["v_ready"], j + 1)
                    if used is not None:
                        dve.wait_ge(S["coef_step"], used)
                    stt(pm[:], half_rows(q2[:, 1], q), 1 + 2 * DT, v[:], ALU.add, ALU.mult, S["pm_ready"])

                def coefficient(j, p, c):
                    done = S["coef_step"]

                    def after(k):
                        dve.wait_ge(done, j * COEF + k)

                    def both(ap):
                        return ap.unsqueeze(1).broadcast_to(pair_shape)

                    if c == 1:
                        dve.wait_ge(S["rcp0_ready"], j + 1)
                        dve.wait_ge(S["pm_ready"], j + 1)
                        stt(tnewton[:], pm[:], -2 * DT, rcp[:], ALU.add, ALU.mult, done)
                    if c == 2:
                        after(1)
                        stt(rcp[:], tnewton[:], 2.0, rcp[:], ALU.subtract, ALU.mult, done, reverse0=True)
                    if c == 3:
                        after(2)
                        stt(xy[:], q2[:, :, UR * p:UR * (p + 1)], 1.0, both(rcp[:]), ALU.add, ALU.mult, done)
                    if c == 4:
                        after(3)
                        tt(one_minus_d[:], xy[:, 0], xy[:, 1], ALU.add, done)
                    if c in (5, 6):
                        after(4)
                        stt(minus_dab[:, c - 5], one_minus_d[:], -1.0, ab[:, c - 5, UR * p:UR * (p + 1), inner], ALU.add, ALU.mult, done)
                    if c == 7:
                        dve.wait_ge(S["self_done"], j + 1)
                        stt(co[p]["self"][:], one_minus_d[:], -1.0, kbank[:], ALU.add, ALU.mult, done)
                    if c == 8:
                        after(6)
                        tt(co[p]["cross"][:, 0], xy[:], minus_dab[:], ALU.add, done)
                    if c == 9:
                        tt(co[p]["cross"][:, 1], xy[:], minus_dab[:], ALU.subtract, done)
                    if c == 10:
                        dve.wait_ge(S["f_ready"], j * 3 + 1)
                        stt(co[p]["src"][:], one_minus_d[:], -1.0, f[p][:, :, inner], ALU.add, ALU.mult, done)
                    if c == 11:
                        after(7)
                        dve.wait_ge(S["old_ready"], j * 2 + 2)
                        tt(co[p]["first"][:], co[p]["self"][:], co[p]["first"][:], ALU.add, done)

                def products(j, p, k, between=lambda: None):
                    done = S["products"]
                    h = f[p] if k == 1 else hbuf[(k - 1) % 2]
                    old = f[p] if k == 2 else hbuf[k % 2]
                    m0, c = m_old[(k + p) % 2], co[p]
                    if k == 1:
                        dve.wait_ge(S["coef_step"], (j + 1) * COEF)
                        dve.wait_ge(S["f_ready"], (j + 1) * 3)
                        dve.wait_ge(S["accumulated"], j * STEPS)
                        tt(m0[:], c["first"][:], h[:, :, inner], ALU.mult, done)
                        dve.wait_ge(S["shifted_ready"], (j + 1) * 2)
                    else:
                        dve.wait_ge(S["accumulated"], j * STEPS + k - 2)
                        tt(m0[:], c["old"][:], old[:, :, inner], ALU.mult, done)
                        dve.wait_ge(S["h_ready"], h_count(j, k - 1, 1))
                        tt(prod_self[:], c["self"][:], h[:, :, inner], ALU.mult, done)
                    tt(prod_w[:], c["cross"][:, :, 0], h[:, :, inner].unsqueeze(1).broadcast_to(pair_shape), ALU.mult, done)
                    if k > 1:
                        dve.wait_ge(done, product_count(j, k, 2))
                        tt(m0[:], m0[:], prod_self[:], ALU.add, done)
                        dve.wait_ge(S["h_ready"], h_count(j, k - 1))
                    tt(prod_c[:], c["cross"][:, :, 1], neighbours(h), ALU.mult, done)
                    between()
                    dve.wait_ge(done, product_count(j, k, PRODUCTS[k] - 1))
                    tt(prod_c[:, 0], prod_c[:, 0], prod_c[:, 1], ALU.add, done)

                def last(t, p):
                    j, out, done = t * 2 + p, x1_tile[p], S["last_step"]
                    row = (P, UR, NLON)
                    dve.wait_ge(x1_stored[p], t * 16)
                    dve.wait_ge(S["x1_turned"], j)
                    dve.wait_ge(S["accumulated"], (j + 1) * STEPS)
                    tt(out[:], hbank[:, (STEPS + p) % 2], out_scale[:].unsqueeze(1).broadcast_to(row), ALU.mult, done)
                    dve.wait_ge(done, j * 3 + 1)
                    tt(out[:], out[:], out_bias[:].unsqueeze(1).broadcast_to(row), ALU.add, done)
                    dve.wait_ge(x2_loaded[p], t * 16 + 16)
                    dve.wait_ge(done, j * 3 + 2)
                    stt(out[:], out[:], 0.0, x2[p][:], ALU.max, ALU.add, done)

                def x1_statistics(t, p):
                    dve.wait_ge(S["x1_turned"], t * 2 + p + 1)
                    for h in range(2):
                        nc.vector.bn_stats(
                            out=stats[:, bass.ds(t * 2 + p + h * NU, 1), :].rearrange("p a k -> p (a k)"),
                            in_=turn[:, 2 * h:2 * h + 2].rearrange("p a w -> p (a w)")).then_inc(S["x1_stats"], 1)

                nc.vector.memset(convin[:], 0.0).then_inc(S["padded"], 1)
                nc.vector.memset(minus_04[:], -2 * DT).then_inc(S["padded"], 1)
                norm_scaled(0, 0)
                norm_shifted(0, 0)
                denominator(0, 0)
                for c in range(1, COEF + 1):
                    coefficient(0, 0, c)
                denominator(1, 1, 1)
                norm_scaled(1, 0)
                norm_shifted(1, 0)
                products(0, 0, 1, lambda: coefficient(1, 1, 1))
                with dve.Fori(0, NG) as t:
                    sample = ((t + 2) >> GPS_BITS) & (B - 1)
                    for p in range(2):
                        j = t * 2 + p
                        coefficient(j + 1, 1 - p, 2)
                        coefficient(j + 1, 1 - p, 3)
                        coefficient(j + 1, 1 - p, 4)
                        products(j, p, 2)
                        coefficient(j + 1, 1 - p, 5)
                        coefficient(j + 1, 1 - p, 6)
                        coefficient(j + 1, 1 - p, 7)
                        products(j, p, 3)
                        coefficient(j + 1, 1 - p, 8)
                        coefficient(j + 1, 1 - p, 9)
                        if p == 1:
                            norm_scaled(t + 2, sample)
                        products(j, p, 4)
                        coefficient(j + 1, 1 - p, 10)
                        if p == 1:
                            norm_shifted(t + 2, sample)
                        products(j, p, 5)
                        denominator(j + 2, p, (j + 1) * COEF + 1)
                        coefficient(j + 1, 1 - p, 11)
                        last(t, p)
                        products(j + 1, 1 - p, 1, lambda: coefficient(j + 2, p, 1))
                        x1_statistics(t, p)

            @block.scalar
            def _(act):
                def block_rows(j, q):
                    act.wait_ge(S["norm_step"], norm_count(j, 2))
                    act.wait_ge(S["turned"], j * 2)
                    nc.scalar.copy(blocks4[:], s6[:, UR * q:UR * q + 4].rearrange("p r (g c) -> p g r c", c=CB)) \
                        .then_inc(S["blocks_ready"], 1)

                def f_copy(j, q, used):
                    if used is not None:
                        act.wait_ge(S["products"], used)
                    act.wait_ge(S["norm_step"], norm_count(j, 2))
                    src = s6[:, 1 + UR * q:1 + UR * (q + 1)]
                    nc.scalar.copy(f[q][:, :, inner], src).then_inc(S["f_ready"], 1)
                    nc.scalar.copy(f[q][:, :, 0:1], src[:, :, NLON - 1:NLON]).then_inc(S["f_ready"], 1)
                    nc.scalar.copy(f[q][:, :, NLON + 1:W2], src[:, :, 0:1]).then_inc(S["f_ready"], 1)

                def convin_copy(j, q, h, group):
                    act.wait_ge(S["padded"], 2)
                    act.wait_ge(S["turned"], j * 2 + h + 1)
                    act.wait_ge(S["conv_done"], j * 2)
                    nc.scalar.activation(convin[:, 4 * h:4 * h + 4, 1:P + 1], turn[:], ACT.Copy,
                                         scale=row_mask[:, q, bass.ds(group, 1)]).then_inc(S["convin_ready"], 1)

                def relu(j, q, h):
                    act.wait_ge(S["conv_done"], j * 2 + h + 1)
                    if not isinstance(j, int):
                        act.wait_ge(S["coef_step"], (j - 1) * COEF)
                    nc.scalar.activation(ab[:, :, UR * q:UR * (q + 1), 1 + h * HALF:1 + (h + 1) * HALF],
                                         cbank[:, h], ACT.Relu).then_inc(S["relu_done"], 1)

                def pads_ab(j, q):
                    act.wait_ge(S["relu_done"], j * 2 + 2)
                    b = ab[:, 1, UR * q:UR * (q + 1)]
                    nc.scalar.copy(b[:, :, 0:1], b[:, :, NLON:NLON + 1]).then_inc(S["pads_ab"], 1)
                    nc.scalar.copy(b[:, :, NLON + 1:W2], b[:, :, 1:2]).then_inc(S["pads_ab"], 1)

                def squares(j, q):
                    act.wait_ge(S["sobel_done"], j + 1)
                    if not isinstance(j, int):
                        act.wait_ge(S["coef_step"], (j - 1) * COEF)
                    for a in range(2):
                        nc.scalar.activation(half_rows(q2[:, a], q), sbank[:, a], ACT.Square, scale=0.5).then_inc(S["squares_done"], 1)

                def v_of(j, q):
                    act.wait_ge(S["squares_done"], j * 2 + 2)
                    act.wait_ge(S["pm_ready"], j)
                    nc.scalar.activation(v[:], half_rows(q2[:, 0], q), ACT.Copy, scale=2.5, bias=2.5 * (1 + 2 * DT)).then_inc(S["v_ready"], 1)

                def reciprocal(j, used):
                    act.wait_ge(S["pm_ready"], j + 1)
                    if used is not None:
                        act.wait_ge(S["coef_step"], used)
                    nc.scalar.activation(rcp[:], pm[:], ACT.Ln, bias=minus_04[:, 0:1]).then_inc(S["ln_done"], 1)
                    act.wait_ge(S["ln_done"], j + 1)
                    nc.scalar.activation(rcp[:], rcp[:], ACT.Exp, scale=-1.0).then_inc(S["rcp0_ready"], 1)

                def old_coefficient(j, p):
                    act.wait_ge(S["coef_step"], j * COEF + 4)
                    nc.scalar.activation(co[p]["old"][:], one_minus_d[:], ACT.Copy, scale=-2.0, bias=1.0).then_inc(S["old_ready"], 1)
                    nc.scalar.activation(co[p]["first"][:], one_minus_d[:], ACT.Copy, scale=-2.0 - 2 * DT, bias=1.0 + 2 * DT) \
                        .then_inc(S["old_ready"], 1)

                def shifted(j, p, sides=(0, 1)):
                    for i in sides:
                        act.wait_ge(S["shift_done"], j * 2 + i + 1)
                        nc.scalar.copy(co[p]["cross"][:, i, 0], kbank[:]).then_inc(S["shifted_ready"], 1)

                def evacuate(j, p, k):
                    h, bank = hbuf[k % 2], hbank[:, (k + p) % 2]
                    act.wait_ge(S["accumulated"], j * STEPS + k)
                    nc.scalar.copy(h[:, :, inner], bank).then_inc(S["h_ready"], 1)
                    nc.scalar.copy(h[:, :, 0:1], bank[:, :, NLON - 1:NLON]).then_inc(S["h_ready"], 1)
                    nc.scalar.copy(h[:, :, NLON + 1:W2], bank[:, :, 0:1]).then_inc(S["h_ready"], 1)

                nc.scalar.preload_act_table_set("natural_log_exp_and_others")
                block_rows(0, 0)
                for j in range(2):
                    if j == 1:
                        block_rows(1, 1)
                    convin_copy(j, j, 0, 0)
                    squares(j, j)
                    v_of(j, j)
                    convin_copy(j, j, 1, 0)
                    relu(j, j, 0)
                    relu(j, j, 1)
                    pads_ab(j, j)
                    f_copy(j, j, None)
                    reciprocal(j, COEF if j else None)
                    if j == 1:
                        block_rows(2, 0)
                    if j == 0:
                        old_coefficient(0, 0)
                        shifted(0, 0)
                with act.Fori(0, NG) as t:
                    for p in range(2):
                        j = t * 2 + p
                        group = (t + 1) & (GPS - 1)
                        evacuate(j, p, 1)
                        convin_copy(j + 2, p, 0, group)
                        old_coefficient(j + 1, 1 - p)
                        evacuate(j, p, 2)
                        f_copy(j + 2, p, product_count(j, 2))
                        squares(j + 2, p)
                        v_of(j + 2, p)
                        evacuate(j, p, 3)
                        convin_copy(j + 2, p, 1, group)
                        shifted(j + 1, 1 - p, (0,))
                        evacuate(j, p, 4)
                        shifted(j + 1, 1 - p, (1,))
                        block_rows(j + 3, 1 - p)
                        relu(j + 2, p, 0)
                        reciprocal(j + 2, (j + 1) * COEF + 3)
                        relu(j + 2, p, 1)
                        pads_ab(j + 2, p)

            @block.tensor
            def _(pe):
                def turns(j, h, stats_used=None):
                    pe.wait_ge(S["blocks_ready"], j + 1)
                    pe.wait_ge(S["convin_ready"], j * 2 + h)
                    if stats_used is not None:
                        pe.wait_ge(S["x1_stats"], stats_used)
                    for g in range(4):
                        mm = nc.tensor.transpose(turn[:, g], blocks4[:, 4 * h + g].rearrange("p r c -> p (r c)"), mat("eye"))
                    mm.then_inc(S["turned"], 1)

                def conv(j, h):
                    pe.wait_ge(S["convin_ready"], j * 2 + h + 1)
                    pe.wait_ge(S["relu_done"], j * 2)
                    nc.tensor.matmul(cbank[:, h].rearrange("p k r c -> p (k r c)"), row_pick[:],
                                     conv_bias[:, h].rearrange("p k r c -> p (k r c)"), start=True, stop=False, skip_group_check=True)
                    for g4 in range(NB_ // 2):
                        g = h * (NB_ // 2) + g4
                        for dx in range(3):
                            mm = nc.tensor.matmul(cbank[:, h, :, :, g4 * CB:(g4 + 1) * CB], convin[:, g, dx:dx + P], conv_w[:, g, dx],
                                                  start=False, stop=(g4 == NB_ // 2 - 1 and dx == 2), skip_group_check=True)
                    mm.then_inc(S["conv_done"], 1)

                def sobel(j, q):
                    pe.wait_ge(S["norm_step"], norm_count(j, NORM))
                    pe.wait_ge(S["squares_done"], j * 2)
                    gx, gy = sbank[:, 0], sbank[:, 1]

                    def rows(i):
                        return s6[:, UR * q + i:UR * q + i + UR]
                    nc.tensor.matmul(gy, mat("smooth"), rows(2), start=True, stop=False)
                    nc.tensor.matmul(gy, mat("minus_smooth"), rows(0), start=False, stop=True)
                    nc.tensor.matmul(gx, mat("slope2"), rows(1), start=True, stop=False)
                    nc.tensor.matmul(gx, mat("slope"), half_rows(row_sum, q), start=False, stop=True).then_inc(S["sobel_done"], 1)

                def self_term(j, q):
                    pe.wait_ge(S["pads_ab"], j * 2 + 2)
                    pe.wait_ge(S["relu_done"], j * 2 + 2)
                    pe.wait_ge(S["shifted_ready"], j * 2)
                    a, b = ab[:, 0, UR * q:UR * (q + 1)], ab[:, 1, UR * q:UR * (q + 1)]
                    nc.tensor.matmul(kbank[:], mat("prev_minus_next"), a[:, :, inner], start=True, stop=False)
                    nc.tensor.matmul(kbank[:], mat("minus_eye"), b[:, :, 2:NLON + 2], start=False, stop=False)
                    nc.tensor.matmul(kbank[:], mat("eye"), b[:, :, 0:NLON], start=False, stop=True).then_inc(S["self_done"], 1)

                def shift_prev(j, p):
                    pe.wait_ge(S["coef_step"], j * COEF + 8)
                    nc.tensor.matmul(kbank[:], mat("from_next"), co[p]["cross"][:, 0, 0], start=True, stop=True).then_inc(S["shift_done"], 1)

                def shift_next(j, p):
                    pe.wait_ge(S["coef_step"], j * COEF + 9)
                    pe.wait_ge(S["shifted_ready"], j * 2 + 1)
                    nc.tensor.matmul(kbank[:], mat("from_prev"), co[p]["cross"][:, 1, 0], start=True, stop=True).then_inc(S["shift_done"], 1)

                def accumulate(j, p, k):
                    out, c = hbank[:, (k + p) % 2], co[p]
                    if k == 1:
                        pe.wait_ge(S["h_ready"], h_count(j, 0))
                    else:
                        if k == 2:
                            pe.wait_ge(S["coef_step"], j * COEF + 10)
                            pe.wait_ge(S["last_step"], j * 3)
                        else:
                            pe.wait_ge(S["h_ready"], h_count(j, k - 2))
                        nc.tensor.matmul(out, mat("source"), c["src"][:], start=True, stop=False)

                    def own(i):
                        pe.wait_ge(S["products"], product_count(j, k, i))
                        nc.tensor.matmul(out, mat("eye"), m_old[(k + p) % 2][:], start=(k == 1), stop=False)

                    if k == 1:
                        own(1)
                    pe.wait_ge(S["products"], product_count(j, k, 2 if k == 1 else 3))
                    nc.tensor.matmul(out, mat("from_prev"), prod_w[:, 0], start=False, stop=False)
                    nc.tensor.matmul(out, mat("from_next"), prod_w[:, 1], start=False, stop=False)
                    if k > 1:
                        own(4)
                    pe.wait_ge(S["products"], product_count(j, k))
                    nc.tensor.matmul(out, mat("eye"), prod_c[:, 0], start=False, stop=True).then_inc(S["accumulated"], 1)

                def turn_x1(j, p):
                    pe.wait_ge(S["last_step"], j * 3 + 3)
                    pe.wait_ge(S["convin_ready"], j * 2 + 6)
                    for h in range(2):
                        for r in range(UR):
                            mm = nc.tensor.transpose(turn[:, UR * h + r], x1_tile[p][:, r, h * HALF:(h + 1) * HALF], mat("eye"))
                    mm.then_inc(S["x1_turned"], 1)

                for j in range(2):
                    turns(j, 0)
                    sobel(j, j)
                    turns(j, 1)
                    conv(j, 0)
                    conv(j, 1)
                    if j == 0:
                        self_term(0, 0)
                        shift_prev(0, 0)
                        shift_next(0, 0)
                with pe.Fori(0, NG) as t:
                    for p in range(2):
                        j = t * 2 + p
                        accumulate(j, p, 1)
                        self_term(j + 1, 1 - p)
                        turns(j + 2, 0, j * 2)
                        accumulate(j, p, 2)
                        sobel(j + 2, p)
                        accumulate(j, p, 3)
                        turns(j + 2, 1)
                        shift_prev(j + 1, 1 - p)
                        accumulate(j, p, 4)
                        shift_next(j + 1, 1 - p)
                        if p == 1:
                            conv(j + 2, 0)
                        accumulate(j, p, 5)
                        if p == 0:
                            conv(j + 2, 0)
                            turn_x1(j, p)
                        conv(j + 2, 1)
                        if p == 1:
                            turn_x1(j, p)

        group_norm_scales("_x1", SAMPLE_ROWS // 2)
        stats_scope.close()

        L = MODES
        RI_M = 2 * MODES
        with ExitStack() as layer_scope:
            sb, _, _ = alloc(layer_scope)
            spec = sb("spec", [P, L, MODES, 2, B])

            with ExitStack() as scope:
                sb, ps, sem = alloc(scope)
                legendre = sb("an_legendre", [L, MODES, P])
                dft = sb("dft", [P, 2, RI_M])
                quad = sb("quad", [P, 1])
                analysis = sb("analysis", [P, MODES, L])
                rows = [sb(f"an_rows{i}", [P, RG, NLON]) for i in range(2)]
                normed = [sb(f"an_normed{i}", [P, 2, RG * P]) for i in range(2)]
                now = sb("an_now", [P, 2, 2])
                fourier = sb("fourier", [P, P, RI_M])
                turned = [ps(f"an_turned{i}", [P, 2, RG * P]) for i in range(2)]
                fbank = [ps(f"fbank{i}", [P, 512]) for i in range(2)]
                lbank = [ps(f"lbank{i}", [P, MODES // 2, L]) for i in range(2)]
                names = "const_loaded now_ready turned_done normed_done dft_done fourier_done legendre_done spec_done pct_turned pct_ready".split()
                S = {k: sem("an_" + k) for k in names}
                rows_loaded = [sem(f"an_rows_loaded{i}") for i in range(2)]
                block = scope.enter_context(nc.Block(name="analysis"))
                PAIRS = GPS // 2

                @block.sync
                def _(sp):
                    sp.dma_start(dft[:], c_dft).then_inc(S["const_loaded"], 16)
                    sp.dma_start(quad[:], quad_w.rearrange("(t a) -> t a", a=1)).then_inc(S["const_loaded"], 16)
                    sp.dma_start(legendre[:], pct[0:L, 0:MODES, :]).then_inc(S["const_loaded"], 16)
                    for i in range(2):
                        sp.dma_start(rows[i][:], x1_rows[:, i * RG:(i + 1) * RG, :]).then_inc(rows_loaded[i], 16)
                    with sp.Fori(0, NG // 2 - 1) as t:
                        for i in range(2):
                            sp.wait_ge(S["turned_done"], t * 2 + i + 1)
                            sp.dma_start(rows[i][:], x1_rows[:, bass.ds((t * 2 + 2 + i) * RG, RG), :]) \
                                .then_inc(rows_loaded[i], 16)

                @block.tensor
                def _(pe):
                    pe.wait_ge(S["const_loaded"], 48)
                    for m in range(MODES):
                        if m == MODES // 2:
                            pe.wait_ge(S["pct_ready"], 1)
                        k = m % (MODES // 2)
                        mm = nc.tensor.transpose(fbank[0][:, k * L:(k + 1) * L], legendre[:, m, :], mat("eye")[0:L, 0:L])
                        if k == MODES // 2 - 1:
                            mm.then_inc(S["pct_turned"], 1)
                    pe.wait_ge(S["pct_ready"], 2)

                    def turn(i, t):
                        pe.wait_ge(rows_loaded[i], t * 16 + 16)
                        pe.wait_ge(S["normed_done"], t * 4)
                        for r in range(RG):
                            for h in range(2):
                                mm = nc.tensor.transpose(turned[i][:, h, r * P:(r + 1) * P],
                                                         rows[i][:, r, h * HALF:(h + 1) * HALF], mat("eye"))
                        mm.then_inc(S["turned_done"], 1)

                    def fourier_of(i, t):
                        pe.wait_ge(S["normed_done"], t * 4 + 2 * i + 2)
                        pe.wait_ge(S["fourier_done"], t * 2)
                        for r in range(RG):
                            for h in range(2):
                                mm = nc.tensor.matmul(fbank[i][:, r * RI_M:(r + 1) * RI_M], normed[i][:, h, r * P:(r + 1) * P],
                                                      dft[:, h, :], start=(h == 0), stop=(h == 1), skip_group_check=True)
                        mm.then_inc(S["dft_done"], 1)

                    with pe.Fori(0, B) as b:
                        with pe.Fori(0, PAIRS) as j:
                            t = b * PAIRS + j
                            turn(0, t)
                            turn(1, t)
                            fourier_of(0, t)
                            fourier_of(1, t)
                        pe.wait_ge(S["fourier_done"], (b + 1) * GPS)
                        for k in range(4):
                            ri, mh = k // 2, k % 2
                            pe.wait_ge(S["spec_done"], b * 4 + (0, 0, 1, 2)[k])
                            for m in range(MODES // 2):
                                mode = mh * (MODES // 2) + m
                                mm = nc.tensor.matmul(lbank[k % 2][:, m, :], fourier[:, :, ri * MODES + mode],
                                                      analysis[:, mode, :], start=True, stop=True)
                            mm.then_inc(S["legendre_done"], 1)

                @block.scalar
                def _(act):
                    act.wait_ge(S["const_loaded"], 48)
                    for m in range(2):
                        act.wait_ge(S["pct_turned"], m + 1)
                        nc.scalar.activation(analysis[:, m * (MODES // 2):(m + 1) * (MODES // 2), :],
                                             fbank[0][:].rearrange("p (m l) -> p m l", l=L), ACT.Copy, scale=quad[:, 0:1]) \
                            .then_inc(S["pct_ready"], 1)
                    with act.Fori(0, B) as b:
                        with act.Fori(0, PAIRS) as j:
                            t = b * PAIRS + j
                            act.wait_ge(S["now_ready"], b * 2 + 2)
                            for i in range(2):
                                act.wait_ge(S["turned_done"], t * 2 + i + 1)
                                act.wait_ge(S["dft_done"], t * 2)
                                for h in range(2):
                                    nc.scalar.activation(normed[i][:, h, :], turned[i][:, h, :], ACT.Identity,
                                                         scale=now[:, 0, h:h + 1], bias=now[:, 1, h:h + 1]) \
                                        .then_inc(S["normed_done"], 1)

                @block.vector
                def _(dve):
                    with dve.Fori(0, B) as b:
                        dve.wait_ge(S["normed_done"], b * (2 * GPS))
                        for k, g in enumerate((gn_scale, gn_bias)):
                            nc.vector.tensor_scalar(now[:, k, :], g[:, bass.ds(b, 1), :].rearrange("p a h -> p (a h)"),
                                                    1.0, None, ALU.mult).then_inc(S["now_ready"], 1)
                        with dve.Fori(0, PAIRS) as j:
                            dve.wait_ge(S["legendre_done"], b * 4)
                            t = b * PAIRS + j
                            for i in range(2):
                                dve.wait_ge(S["dft_done"], t * 2 + i + 1)
                                nc.vector.tensor_copy(fourier[:, bass.ds((j * 2 + i) * RG, RG), :],
                                                      fbank[i][:, 0:RG * RI_M].rearrange("p (r k) -> p r k", k=RI_M)) \
                                    .then_inc(S["fourier_done"], 1)
                        for k in range(4):
                            ri, mh = k // 2, k % 2
                            modes = slice(mh * (MODES // 2), (mh + 1) * (MODES // 2))
                            dve.wait_ge(S["legendre_done"], b * 4 + k + 1)
                            out = spec[:, :, modes, ri, bass.ds(b, 1)].rearrange("p l m a -> p m l a")[:, :, :, 0]
                            nc.vector.tensor_copy(out, lbank[k % 2][:]).then_inc(S["spec_done"], 1)

            with ExitStack() as scope:
                sb, ps, sem = alloc(scope)
                LL = 2
                wl = [sb(f"wl{i}", [P, P, LL, RI_M]) for i in range(2)]
                obank = [[ps(f"obank{l}_{c}", [P, MODES, 2, B]) for c in range(2)] for l in range(LL)]
                w_loaded = [sem(f"w_loaded{i}") for i in range(2)]
                mixed, mixed_out = sem("mixed"), sem("mixed_out")
                block = scope.enter_context(nc.Block(name="mixing"))
                w_rows = weights.rearrange("i o l m c -> i o l (m c)")
                LOADS = L // LL
                OUT_STEPS = 3

                @block.sync
                def _(sp):
                    with sp.Fori(0, LOADS // 2) as t:
                        for i in range(2):
                            sp.wait_ge(mixed, t * (2 * LL))
                            sp.dma_start(wl[i][:], w_rows[:, :, bass.ds((t * 2 + i) * LL, LL), :]).then_inc(w_loaded[i], 16)

                @block.tensor
                def _(pe):
                    with pe.Fori(0, LOADS // 2) as t:
                        for i in range(2):
                            pe.wait_ge(w_loaded[i], t * 16 + 16)
                            for l in range(LL):
                                pe.wait_ge(mixed_out, (t * 2 + i) * (OUT_STEPS * LL))
                                for m in range(MODES):
                                    part = spec[:, bass.ds((t * 2 + i) * LL + l, 1), m, :, :].rearrange("p a s b -> p (a s b)")
                                    for c in range(2):
                                        mm = nc.tensor.matmul(obank[l][c][:, m].rearrange("p s b -> p (s b)"),
                                                              wl[i][:, :, l, 2 * m + c], part, start=True, stop=True)
                                mm.then_inc(mixed, 1)

                @block.vector
                def _(dve):
                    with dve.Fori(0, LOADS // 2) as t:
                        for i in range(2):
                            for l in range(LL):
                                n = (t * 2 + i) * LL + l
                                out = spec[:, bass.ds(n, 1), :, :, :].rearrange("p a m s b -> p (a m) s b")
                                dve.wait_ge(mixed, n + 1)
                                nc.vector.tensor_copy(out.rearrange("p m s b -> p m (s b)"),
                                                      obank[l][0][:].rearrange("p m s b -> p m (s b)")).then_inc(mixed_out, 1)
                                dve.wait_ge(mixed_out, n * OUT_STEPS + 1)
                                nc.vector.tensor_tensor(out[:, :, 0], out[:, :, 0], obank[l][1][:, :, 1], ALU.subtract).then_inc(mixed_out, 1)
                                nc.vector.tensor_tensor(out[:, :, 1], out[:, :, 1], obank[l][1][:, :, 0], ALU.add).then_inc(mixed_out, 1)

            with ExitStack() as scope:
                sb, ps, sem = alloc(scope)
                legendre = sb("sy_legendre", [L, MODES, P])
                idft = sb("idft", [P, NLON])
                picked = sb("picked", [P, 2, MODES, L])
                by_l = sb("by_l", [L, MODES, 2, P])
                field = sb("field", [P, P, RI_M])
                four = [sb(f"four{i}", [P, RG * RI_M]) for i in range(2)]
                by_mode = [sb(f"by_mode{i}", [P, 2, P]) for i in range(2)]
                NR = 4
                rows = [sb(f"sy_rows{i}", [P, RG, NLON]) for i in range(NR)]
                tb = [ps(f"tb{i}", [P, 512]) for i in range(2)]
                yb = [ps(f"yb{i}", [P, 2, 2, NLON]) for i in range(2)]
                names = "const_loaded picked_done l_turned l_copied z_done z_copied four_done turned copied y_done y_added".split()
                S = {k: sem("sy_" + k) for k in names}
                rows_loaded = [sem(f"sy_rows_loaded{i}") for i in range(NR)]
                stored = [sem(f"sy_stored{i}") for i in range(NR)]
                block = scope.enter_context(nc.Block(name="synthesis"))
                PAIRS = GPS // 2
                NT = 2 * MODES // 4
                NZ = MODES // 2

                @block.sync
                def _(sp):
                    sp.dma_start(legendre[:], pct[0:L, 0:MODES, :]).then_inc(S["const_loaded"], 16)
                    sp.dma_start(idft[:], c_idft).then_inc(S["const_loaded"], 16)
                    with sp.Fori(0, NG // NR) as t:
                        for i in range(NR):
                            sp.wait_ge(stored[i], t * 16)
                            sp.dma_start(rows[i][:], x1_rows[:, bass.ds((t * NR + i) * RG, RG), :]) \
                                .then_inc(rows_loaded[i], 16)

                @block.gpsimd
                def _(pool):
                    with pool.Fori(0, NG // NR) as t:
                        for i in range(NR):
                            pool.wait_ge(S["y_added"], t * (2 * NR) + 2 * i + 2)
                            pool.dma_start(y_rows[:, bass.ds((t * NR + i) * RG, RG), :], rows[i][:]).then_inc(stored[i], 16)
                    for i in range(NR):
                        pool.wait_ge(stored[i], 16 * (NG // NR))

                @block.tensor
                def _(pe):
                    pe.wait_ge(S["const_loaded"], 32)
                    with pe.Fori(0, B) as b:
                        pe.wait_ge(S["picked_done"], b * 2 + 2)
                        pe.wait_ge(S["copied"], b * GPS)
                        for k in range(NT):
                            if k >= 2:
                                pe.wait_ge(S["l_copied"], b * NT + k - 1)
                            for q in range(4):
                                m, ri = divmod(4 * k + q, 2)
                                mm = nc.tensor.transpose(tb[k % 2][0:L, q * P:(q + 1) * P], picked[:, ri, m, :], mat("eye"))
                            mm.then_inc(S["l_turned"], 1)
                        pe.wait_ge(S["l_copied"], (b + 1) * NT)
                        for k in range(NZ):
                            if k >= 2:
                                pe.wait_ge(S["z_copied"], b * NZ + k - 1)
                            for q in range(2):
                                m = 2 * k + q
                                mm = nc.tensor.matmul(tb[k % 2][:, q * NLON:(q + 1) * NLON], legendre[:, m, :],
                                                      by_l[:, m].rearrange("l c o -> l (c o)"), start=True, stop=True)
                            mm.then_inc(S["z_done"], 1)
                        with pe.Fori(0, PAIRS) as j:
                            pe.wait_ge(S["z_copied"], (b + 1) * NZ)
                            t = b * PAIRS + j
                            for i in range(2):
                                pe.wait_ge(S["four_done"], t * 2 + i + 1)
                                pe.wait_ge(S["copied"], t * 2)
                                for p in range(2):
                                    mm = nc.tensor.transpose(tb[i][:, p * P:(p + 1) * P], four[i][:, p * P:(p + 1) * P], mat("eye"))
                                mm.then_inc(S["turned"], 1)
                            for i in range(2):
                                pe.wait_ge(S["copied"], t * 2 + i + 1)
                                pe.wait_ge(S["y_added"], t * 4)
                                for p in range(2):
                                    for o in range(2):
                                        q = slice(RI_M * o, RI_M * (o + 1))
                                        mm = nc.tensor.matmul(yb[i][:, o, p], by_mode[i][q, p, :], idft[q, :], start=True, stop=True)
                                mm.then_inc(S["y_done"], 1)

                @block.scalar
                def _(act):
                    with act.Fori(0, B) as b:
                        act.wait_ge(S["l_turned"], b * NT)
                        for ri in range(2):
                            nc.scalar.copy(picked[:, ri], spec[:, :, :, ri, bass.ds(b, 1)]
                                           .rearrange("p l m a -> p m l a")[:, :, :, 0]).then_inc(S["picked_done"], 1)
                        act.wait_ge(S["z_done"], b * NZ)
                        for k in range(NT):
                            act.wait_ge(S["l_turned"], b * NT + k + 1)
                            nc.scalar.copy(by_l[:, 2 * k:2 * k + 2].rearrange("l m c o -> l (m c o)"), tb[k % 2][0:L, :]) \
                                .then_inc(S["l_copied"], 1)
                        act.wait_ge(S["four_done"], b * GPS)
                        for k in range(NZ):
                            act.wait_ge(S["z_done"], b * NZ + k + 1)
                            nc.scalar.copy(field[:].rearrange("t o (c m) -> t m c o", c=2)[:, 2 * k:2 * k + 2],
                                           tb[k % 2][:].rearrange("t (m c o) -> t m c o", m=2, c=2)).then_inc(S["z_copied"], 1)
                        act.wait_ge(S["z_copied"], (b + 1) * NZ)
                        with act.Fori(0, PAIRS) as j:
                            t = b * PAIRS + j
                            for i in range(2):
                                act.wait_ge(S["turned"], t * 2)
                                nc.scalar.copy(four[i][:], field[:, bass.ds((j * 2 + i) * RG, RG), :].rearrange("t o k -> t (o k)")) \
                                    .then_inc(S["four_done"], 1)
                            for i in range(2):
                                act.wait_ge(S["turned"], t * 2 + i + 1)
                                act.wait_ge(S["y_done"], t * 2)
                                nc.scalar.copy(by_mode[i][:].rearrange("k p t -> k (p t)"), tb[i][:, 0:2 * P]).then_inc(S["copied"], 1)

                @block.vector
                def _(dve):
                    with dve.Fori(0, NG // NR) as t:
                        for i in range(NR):
                            dve.wait_ge(rows_loaded[i], t * 16 + 16)
                            dve.wait_ge(S["y_done"], t * NR + i + 1)
                            for o in range(2):
                                def of(a):
                                    return a[:].rearrange("t (p o) n -> t o p n", o=2)[:, o]
                                nc.vector.tensor_tensor(of(rows[i]), yb[i % 2][:, o], of(rows[i]), ALU.add).then_inc(S["y_added"], 1)


_PARAMS = ["wg", "wg1"] + [f"{p}_{q}" for p in ("g", "g1", "out") for q in ("gamma", "beta", "mean", "var")]
_INS = ["x"] + ["L0_conv_" + p for p in _PARAMS] + ["L1_conv_weights", "L1_conv_pct", "L1_conv_w"]


def kernel(**inputs):
    import concourse.bacc as bacc
    from concourse.bass_utils import run_bass_kernel_spmd

    nc = bacc.Bacc("TRN2", target_bir_lowering=False, num_devices=1)
    constants, mat_names = shape_constants()
    arrays = {f"in_{k}": np.ascontiguousarray(inputs[k]) for k in _INS}
    arrays.update({f"const_{k}": v for k, v in constants.items()})
    args = [nc.dram_tensor(k, v.shape, mybir.dt.from_np(v.dtype), kind="ExternalInput").ap() for k, v in arrays.items()]
    y = nc.dram_tensor("y", arrays["in_x"].shape, F32, kind="ExternalOutput").ap()
    build(nc, *args, mat_names, y)
    return run_bass_kernel_spmd(nc, [arrays], core_ids=[0]).results[0]["y"]
```
